# Optimizing a Trainium2 kernel written in Bass

```python
import numpy as np
import jax
import jax.numpy as jnp

def _softmax(x, axis=-1):
    return jax.nn.softmax(x, axis=axis)

def _gelu(x):
    return jax.nn.gelu(x, approximate=True)

def _silu(x):
    return jax.nn.silu(x)

def _sigmoid(x):
    return jax.nn.sigmoid(x)

def _layernorm(x, axis=-1, eps=1e-05):
    m = jnp.mean(x, axis=axis, keepdims=True)
    v = jnp.var(x, axis=axis, keepdims=True)
    return (x - m) / jnp.sqrt(v + eps)

def _scatter_add(tgt, idx, src, axis=0):
    return tgt.at[idx].add(src)

def _segment_sum(src, seg, n):
    return jax.ops.segment_sum(src, seg, n)
kernel_name = 'mk_seq_postln_d1_jaxref_r8_a45d28'

def setup_inputs(seed: int=0):
    np.random.seed(seed)
    _w = jnp.asarray

    def _L0_attn_setup():
        import jax, jax.numpy as jnp
        import numpy as np
        HEADS = 16
        DIM_HEAD = 64
        EPS = 1e-08
        key = jax.random.key(seed)
        ks = jax.random.split(key, 5)
        B, N, D = (2, 256, 128)
        inner = HEADS * DIM_HEAD
        return {'x': jax.random.normal(ks[0], (B, N, D), jnp.float32), 'Wq': jax.random.normal(ks[1], (D, inner), jnp.float32) * D ** (-0.5), 'Wkv': jax.random.normal(ks[2], (D, 2 * inner), jnp.float32) * D ** (-0.5), 'Wo': jax.random.normal(ks[3], (inner, D), jnp.float32) * inner ** (-0.5), 'bo': jax.random.normal(ks[4], (D,), jnp.float32) * 0.02}
    _L0_attn_in = _L0_attn_setup()

    def _L0_ffn_setup():
        import jax, jax.numpy as jnp
        import numpy as np
        DIM = 128

        def _reference_tuple_inner(x, W_r, W_k, W_v, mu_r, mu_k):
            B, T, C = x.shape
            x_prev = jnp.concatenate([jnp.zeros((B, 1, C), x.dtype), x[:, :-1, :]], axis=1)
            xr = mu_r * x + (1.0 - mu_r) * x_prev
            xk = mu_k * x + (1.0 - mu_k) * x_prev
            r = jax.nn.sigmoid(jnp.einsum('btc,dc->btd', xr, W_r))
            k = jnp.einsum('btc,dc->btd', xk, W_k)
            k_act = jnp.square(jax.nn.relu(k))
            out = r * jnp.einsum('btc,dc->btd', k_act, W_v)
            new_state = x[:, -1, :]
            return (out, new_state)
        key = jax.random.key(seed)
        ks = jax.random.split(key, 6)
        B, T, C = (8, 256, DIM)
        x = jax.random.normal(ks[0], (B, T, C), dtype=jnp.float32)
        s = 1.0 / np.sqrt(C)
        W_r = jax.random.uniform(ks[1], (C, C), jnp.float32, -s, s)
        W_k = jax.random.uniform(ks[2], (C, C), jnp.float32, -s, s)
        W_v = jax.random.uniform(ks[3], (C, C), jnp.float32, -s, s)
        mu_r = jax.random.uniform(ks[4], (C,), jnp.float32)
        mu_k = jax.random.uniform(ks[5], (C,), jnp.float32)
        return {'x': x, 'W_r': W_r, 'W_k': W_k, 'W_v': W_v, 'mu_r': mu_r, 'mu_k': mu_k}
    _L0_ffn_in = _L0_ffn_setup()
    _d = {'L0_attn_x': _L0_attn_in['x'], 'L0_attn_Wq': _L0_attn_in['Wq'], 'L0_attn_Wkv': _L0_attn_in['Wkv'], 'L0_attn_Wo': _L0_attn_in['Wo'], 'L0_attn_bo': _L0_attn_in['bo'], 'L0_ffn_W_r': _L0_ffn_in['W_r'], 'L0_ffn_W_k': _L0_ffn_in['W_k'], 'L0_ffn_W_v': _L0_ffn_in['W_v'], 'L0_ffn_mu_r': _L0_ffn_in['mu_r'], 'L0_ffn_mu_k': _L0_ffn_in['mu_k']}
    _x0 = _d['L0_attn_x']
    _d['L0_attn_x'] = jax.random.normal(jax.random.fold_in(jax.random.key(seed), 1), (4, 1024, 128), dtype=_x0.dtype)
    del _x0
    return _d

def reference(L0_attn_x, L0_attn_Wq, L0_attn_Wkv, L0_attn_Wo, L0_attn_bo, L0_ffn_W_r, L0_ffn_W_k, L0_ffn_W_v, L0_ffn_mu_r, L0_ffn_mu_k):

    def _L0_attn_ref(x, Wq, Wkv, Wo, bo):
        import jax, jax.numpy as jnp
        import numpy as np
        HEADS = 16
        DIM_HEAD = 64
        EPS = 1e-08
        B, N, D = x.shape
        H, Dh = (HEADS, DIM_HEAD)
        scale = Dh ** (-0.5)
        q = (x @ Wq).reshape(B, N, H, Dh).transpose(0, 2, 1, 3)
        kv = x @ Wkv
        k = kv[..., :H * Dh].reshape(B, N, H, Dh).transpose(0, 2, 1, 3)
        v = kv[..., H * Dh:].reshape(B, N, H, Dh).transpose(0, 2, 1, 3)
        s = jnp.einsum('bhid,bhjd->bhij', q * scale, k)
        gm = jax.lax.stop_gradient(jnp.max(s, axis=-1, keepdims=True))
        causal_mask = jnp.triu(jnp.ones((N, N), bool), 1)
        p = jnp.where(causal_mask, 0.0, jnp.exp(s - gm))
        num = jnp.einsum('bhij,bhjd->bhid', p, v)
        out = num / (jnp.sum(p, axis=-1, keepdims=True) + EPS)
        out = out.transpose(0, 2, 1, 3).reshape(B, N, H * Dh)
        return out @ Wo + bo

    def _L0_ffn_ref(x, W_r, W_k, W_v, mu_r, mu_k):
        import jax, jax.numpy as jnp
        import numpy as np
        DIM = 128

        def _reference_tuple_inner(x, W_r, W_k, W_v, mu_r, mu_k):
            B, T, C = x.shape
            x_prev = jnp.concatenate([jnp.zeros((B, 1, C), x.dtype), x[:, :-1, :]], axis=1)
            xr = mu_r * x + (1.0 - mu_r) * x_prev
            xk = mu_k * x + (1.0 - mu_k) * x_prev
            r = jax.nn.sigmoid(jnp.einsum('btc,dc->btd', xr, W_r))
            k = jnp.einsum('btc,dc->btd', xk, W_k)
            k_act = jnp.square(jax.nn.relu(k))
            out = r * jnp.einsum('btc,dc->btd', k_act, W_v)
            new_state = x[:, -1, :]
            return (out, new_state)
        return _reference_tuple_inner(x, W_r, W_k, W_v, mu_r, mu_k)[0]
    x = L0_attn_x
    x = _layernorm(x + _L0_attn_ref(x, L0_attn_Wq, L0_attn_Wkv, L0_attn_Wo, L0_attn_bo), axis=-1)
    x = _layernorm(x + _L0_ffn_ref(x, L0_ffn_W_r, L0_ffn_W_k, L0_ffn_W_v, L0_ffn_mu_r, L0_ffn_mu_k), axis=-1)
    return x

_drawn_inputs = setup_inputs


def setup_inputs(seed=0):
    import zlib

    import numpy as np

    out = dict(_drawn_inputs(seed))
    spreads = {}
    factors = {'L0_attn_bo': 2.765, 'L0_ffn_W_r': 3.168, 'L0_ffn_mu_r': 6.253}
    for name, (base, spread) in spreads.items():
        noise = np.random.default_rng([zlib.crc32(name.encode()), seed]).standard_normal(out[name].shape)
        drawn = base * np.exp(spread * noise) if base else spread * noise
        out[name] = jnp.asarray(drawn.astype(out[name].dtype))
    for name, factor in factors.items():
        out[name] = (out[name] * factor).astype(out[name].dtype)
    return out
```

```python
from contextlib import ExitStack

import concourse.bass as bass
from concourse import mybir

F32 = mybir.dt.float32
F32R = mybir.dt.float32r
ALU = mybir.AluOpType
ACT = mybir.ActivationFunctionType

P = 128
B, N, C = 4, 1024, 128
HEADS, DH = 16, 64
TILES = N // P
PAIRS = HEADS // 2
ALL_PAIRS = B * PAIRS
SLOTS = 2 * TILES
HALF = N // 2
SCALE = DH ** -0.5
EPS_SUM = 1e-8
EPS_LN = 1e-5
TURN_LAG = 3
RING = 4
MASKED = 3.0e38

QUADS = [(t, j, min(4, t + 1 - j)) for t in range(TILES) for j in range(0, t + 1, 4)]
NQ = len(QUADS)
FIRST_QUAD = [next(n for n, q in enumerate(QUADS) if q[0] == t) for t in range(TILES)] + [NQ]

PV_AT = {
    8: (0, 0, (0, 1), False), 9: (0, 0, (2, 3), False),
    12: (0, 1, (0, 1, 2), False), 13: (0, 1, (3, 4), False), 14: (0, 1, (5, 6, 7), False),
    0: (1, 0, (0, 1), True), 1: (1, 0, (2, 3), True),
    4: (1, 1, (0, 1, 2), True), 5: (1, 1, (3, 4), True), 6: (1, 1, (5, 6, 7), True),
}
PROJECT_AT = {1: (0, 0), 2: (0, 1), 3: (1, 0), 4: (1, 1), 9: (2, 0), 10: (2, 1)}
PROJECTIONS = list(PROJECT_AT.values())
PROJECTION_OF_SLOT = {k: n for n, k in enumerate(PROJECT_AT)}
NPROJ = len(PROJECTIONS)
OUT_AT = {12: 0, 14: 1}
NORM_AT = {13: (0, 0, False), 15: (0, 1, False), 6: (1, 0, True), 7: (1, 1, True)}


def norms_before(b, half):
    return max(2 * b - 1, 0) if half == 0 else min(2 * b + 2, 2 * B - 1)


def at_least(eng, sem, value):
    if isinstance(value, int) and value <= 0:
        return
    eng.wait_ge(sem, value)


SHARED = []
for _k in range(SLOTS):
    _a, _t = divmod((_k - TURN_LAG) % SLOTS, TILES)
    SHARED += [("quad", _k, _a * NQ + _q) for _q in range(FIRST_QUAD[_t], FIRST_QUAD[_t + 1])]
    if _k in PROJECT_AT:
        SHARED.append(("project", _k, PROJECTION_OF_SLOT[_k]))
    if _k in OUT_AT:
        SHARED.append(("out", _k, OUT_AT[_k]))
NSHARED = 3
BANK = {(kind, n): at % NSHARED for at, (kind, _, n) in enumerate(SHARED)}


def build(nc, x, wq, wkv, wo, bo, w_r, w_k, w_v, mu_r, mu_k, out):
    x_dram = nc.dram_tensor("x_split", [B, P, 2, N], F32).ap()
    w_dram = nc.dram_tensor("w_split", [PAIRS, P, 3, 2, P], F32).ap()
    r_dram = nc.dram_tensor("recips", [2, N], F32).ap()

    with ExitStack() as ctx:
        def sb(name, shape, dt=F32):
            return ctx.enter_context(nc.sbuf_tensor(name, shape, dt))

        def psum(name, shape):
            return ctx.enter_context(nc.psum_tensor(name, shape, F32))

        def sem(name):
            return ctx.enter_context(nc.semaphore(name))

        ident = sb("ident", [P, P])
        xs = sb("xs", [P, 2, N], F32R)
        ws = sb("ws", [P, 3, 2, P], F32R)
        wos = sb("wos", [P, 2, P])
        stage_q = sb("stage_q", [P, 2, N], F32R)
        stage_k = sb("stage_k", [P, 2, N], F32R)
        qs = sb("qs", [P, 2, 2, N], F32R)
        ks = sb("ks", [P, 2, 2, 2, N], F32R)
        vs = sb("vs", [P, 2, TILES, 2, 2, DH], F32R)
        tile = sb("tile", [P, RING, N])
        neg_max = sb("neg_max", [P, RING])
        sums = sb("sums", [P, 2, TILES])
        sums_eps = sb("sums_eps", [P, 2, TILES])
        recips = sb("recips_sb", [P, 2, TILES])
        pt0 = sb("pt0", [P, 2, 4, HALF], F32R)
        pt1 = sb("pt1", [P, 2, 8, HALF], F32R)
        ot = sb("ot", [P, 2, 2, N])
        rb = sb("rb", [P, 2, N])
        y = sb("y", [P, B * N])
        x1t = sb("x1t", [P, 1 + N])
        full = [x1t[:, 1:1 + HALF], x1t[:, 1 + HALF:1 + N]]
        bo_col = sb("bo_col", [P, 1])
        small = sb("small", [P, 4])
        eps_col = sb("eps_col", [P, 1])
        ffn_t = sb("ffn_t", [P, 3, C])
        stats = sb("stats", [P, TILES, 6])
        mv = [sb(f"mv{n}", [P, TILES, 2]) for n in range(2)]
        dev = [sb(f"dev{n}", [P, TILES]) for n in range(2)]
        rstd = [sb(f"rstd{n}", [P, TILES]) for n in range(2)]

        ps_s = [psum("ps_s0", [P, N]), psum("ps_s1", [P, N])]
        ps_x = [psum(f"ps_x{n}", [P, HALF]) for n in range(NSHARED)]
        ps_t = [bank[:, :].rearrange("p (b i) -> p b i", b=4) for bank in ps_x]
        ps_o = psum("ps_o", [P, HALF])

        w_raw = ot[:, :, :, :].rearrange("p a b n -> p (a b n)")[:, 0:3 * HEADS * DH]
        w_hi = pt1[:, 0, :, :].rearrange("p j n -> p (j n)")[:, 0:3 * HEADS * DH]
        w_lo = pt1[:, 1, :, :].rearrange("p j n -> p (j n)")[:, 0:3 * HEADS * DH]
        x_part = pt0[:, :, :, :].rearrange("p a j n -> p (a j n)").rearrange("p (a h n) -> p a h n", a=2, h=2)

        s_ident = sem("s_ident")
        s_xraw = sem("s_xraw")
        s_wraw = sem("s_wraw")
        s_small = sem("s_small")
        s_xturned = sem("s_xturned")
        s_xhi = sem("s_xhi")
        s_xlo = sem("s_xlo")
        s_xstored = [sem("s_xstored0"), sem("s_xstored1")]
        s_whi = sem("s_whi")
        s_wlo = sem("s_wlo")
        s_wstored = sem("s_wstored")
        s_xs = sem("s_xs")
        s_ws = sem("s_ws")
        s_wo = sem("s_wo")
        s_proj = sem("s_proj")
        s_proj_hi = sem("s_proj_hi")
        s_proj_full = sem("s_proj_full")
        s_proj_lo = sem("s_proj_lo")
        s_qs = sem("s_qs")
        s_ks = sem("s_ks")
        s_scores = sem("s_scores")
        s_evac = sem("s_evac")
        s_masked = sem("s_masked")
        s_exp = sem("s_exp")
        s_turned = sem("s_turned")
        s_hi = sem("s_hi")
        s_lo = sem("s_lo")
        s_pv = sem("s_pv")
        s_ot = sem("s_ot")
        s_eps = sem("s_eps")
        s_recip = sem("s_recip")
        s_rdram = sem("s_rdram")
        s_rb = sem("s_rb")
        s_norm = sem("s_norm")
        s_out = sem("s_out")
        s_yadd = sem("s_yadd")
        s_pool_turn = sem("s_pool_turn")
        s_sp_turn = sem("s_sp_turn")
        s_dve_turn = sem("s_dve_turn")
        f_yt = sem("f_yt")
        f_stats = sem("f_stats")
        f_mv = sem("f_mv")
        f_dev = sem("f_dev")
        f_rstd = sem("f_rstd")
        f_x1 = sem("f_x1")
        f_x1t = sem("f_x1t")
        f_x1c = sem("f_x1c")
        f_prev = sem("f_prev")
        f_mix = sem("f_mix")
        f_k = sem("f_k")
        f_relu = sem("f_relu")
        f_act = sem("f_act")
        f_r = sem("f_r")
        f_sig = sem("f_sig")
        f_v = sem("f_v")
        f_gate = sem("f_gate")
        f_sum = sem("f_sum")
        f_fin = sem("f_fin")
        f_w = sem("f_w")
        f_wt = sem("f_wt")
        f_wc = sem("f_wc")
        f_stored = sem("f_stored")

        def tokens(cols):
            return cols.rearrange("p (t c) -> p t c", t=TILES)

        x1 = [tokens(tile[:, n, :]) for n in (0, 1)]
        gate = [tokens(tile[:, n, :]) for n in (2, 3)]
        mix_r = [ot[:, n, 0, :] for n in (0, 1)]
        mix_k = [ot[:, n, 1, :] for n in (0, 1)]
        relu = [rb[:, n, :] for n in (0, 1)]
        fin = [tokens(y[:, b * N:(b + 1) * N]) for b in range(B)]
        w_ffn = x1t[:, 1:1 + 3 * C].rearrange("p (w c) -> p w c", w=3)

        block = ctx.enter_context(nc.Block())

        def pairs_of(eng, body):
            body(0, 0, 0, True)
            body(0, 1, 1, True)
            with eng.Fori(1, ALL_PAIRS // 2 - 1) as i:
                body(i, 0, 2 * i, True)
                body(i, 1, 2 * i + 1, True)
            body(ALL_PAIRS // 2 - 1, 0, ALL_PAIRS - 2, True)
            body(ALL_PAIRS // 2 - 1, 1, ALL_PAIRS - 1, True)
            body(ALL_PAIRS // 2, 0, ALL_PAIRS, False)

        def last(p):
            return isinstance(p, int) and p >= ALL_PAIRS - 1

        def first(p):
            return isinstance(p, int) and p == 0

        @block.sync
        def _(sp):
            for b in range(B):
                sp.dma_start(tile[:, b, :].rearrange("p (t c) -> p t c", t=TILES),
                             x[b, :, :].rearrange("(t p) c -> p t c", p=P)).then_inc(s_xraw, 16)
            sp.dma_start(w_raw[:, 0:N], wq).then_inc(s_wraw, 16)
            sp.dma_start(w_raw[:, N:3 * N], wkv).then_inc(s_wraw, 16)
            sp.dma_start(bo_col[:, :], bo.rearrange("(p a) -> p a", a=1)).then_inc(s_small, 16)
            sp.dma_start(small[:, 0:1], mu_r.rearrange("(p a) -> p a", a=1)).then_inc(s_small, 16)
            sp.dma_start(small[:, 1:2], mu_k.rearrange("(p a) -> p a", a=1)).then_inc(s_small, 16)

            def load_weights(p):
                src = w_dram[bass.ds(p % PAIRS, 1), :, :, :, :].rearrange("a p w h n -> (a p) w h n")
                sp.dma_start(ws[:, :, :, :].bitcast(F32), src).then_inc(s_ws, 16)

            def load_x(i):
                b = i // 4
                src = x_dram[bass.ds(b, 1), :, :, :].rearrange("a p h n -> (a p) h n")
                sp.dma_start(xs[:, :, :].bitcast(F32), src).then_inc(s_xs, 16)

            def load_wo(p):
                rows = wo[bass.ds((p % PAIRS) * P, P), :].rearrange("(a d) c -> d a c", a=2)
                sp.dma_start(wos[0:DH, :, :], rows).then_inc(s_wo, 16)
                sp.dma_start(wos[DH:P, :, :], rows).then_inc(s_wo, 16)

            def stack_q(p, e):
                sp.wait_ge(s_proj_lo, NPROJ * p + 2)
                for a in range(2):
                    for h in range(2):
                        sp.dma_start(qs[h * DH:(h + 1) * DH, e, a, :].bitcast(F32),
                                     stage_q[a * DH:(a + 1) * DH, h, :].bitcast(F32)).then_inc(s_qs, 16)

            def stack_k(p, e):
                sp.wait_ge(s_proj_lo, NPROJ * p + 4)
                for a in range(2):
                    for h in range(2):
                        sp.dma_start(ks[h * DH:(h + 1) * DH, e, a, :, :].bitcast(F32),
                                     stage_k[a * DH:(a + 1) * DH, :, :].bitcast(F32)).then_inc(s_ks, 16)

            def spread_recips(p, a):
                n = 2 * p + a
                sp.wait_ge(s_recip, n + 1)
                at_least(sp, s_norm, 2 * (n - 2) + 2)
                sp.sem_inc(s_sp_turn, 1)
                sp.dma_start(r_dram[a, :].rearrange("(p t) -> p t", p=P), recips[:, a, :]).then_inc(s_rdram, 16)
                sp.wait_ge(s_rdram, 16 * (n + 1))
                sp.sem_inc(s_sp_turn, 1)
                sp.dma_start(rb[:, a, :], r_dram[a, :].partition_broadcast(P)).then_inc(s_rb, 16)

            for b in range(B):
                sp.wait_ge(s_xlo, b + 1)
                sp.dma_start(x_dram[b], x_part[:, b % 2, :, :].bitcast(F32)).then_inc(s_xstored[b % 2], 16)
            for w in range(3):
                sp.wait_ge(s_wlo, w + 1)
                for h, part in enumerate((w_hi, w_lo)):
                    sp.dma_start(w_dram[:, :, w, h, :].rearrange("a p n -> p a n"),
                                 part[:, w * N:(w + 1) * N].bitcast(F32).rearrange("p (a n) -> p a n", a=PAIRS)
                                 ).then_inc(s_wstored, 16)
            sp.wait_ge(s_xstored[0], 16 * B // 2)
            sp.wait_ge(s_xstored[1], 16 * B // 2)
            sp.wait_ge(s_wstored, 16 * 6)
            load_weights(0)
            load_x(0)
            load_wo(0)
            stack_q(0, 0)
            stack_k(0, 0)
            sp.wait_ge(s_proj, NPROJ)
            load_weights(1)

            def body(i, e, p, live):
                if not first(p):
                    spread_recips(p - 1, 1)
                if not last(p):
                    at_least(sp, s_scores, SLOTS * p)
                    sp.sem_inc(s_sp_turn, 1)
                    stack_q(p + 1, 1 - e)
                    stack_k(p + 1, 1 - e)
                if live:
                    spread_recips(p, 0)
                if not last(p) and not (isinstance(p, int) and p == ALL_PAIRS - 2):
                    sp.wait_ge(s_proj, NPROJ * (p + 2))
                    sp.sem_inc(s_sp_turn, 1)
                    load_weights(p + 2)
                    if e == 0:
                        load_x(i + 1)
                if live and not first(p):
                    sp.wait_ge(s_out, 2 * p)
                    sp.sem_inc(s_sp_turn, 1)
                    load_wo(p)

            pairs_of(sp, body)

            sp.wait_ge(s_proj_lo, NPROJ * ALL_PAIRS)
            for n, w in enumerate((w_r, w_k, w_v)):
                sp.dma_start(w_ffn[:, n, :], w).then_inc(f_w, 16)
            for b in range(B):
                sp.wait_ge(f_fin, b + 1)
                sp.dma_start(out[b, :, :].rearrange("(t p) c -> p t c", p=P), fin[b]).then_inc(f_stored, 16)
            sp.wait_ge(f_stored, 16 * B)

        @block.gpsimd
        def _(pool):
            pool.memset(ident[:, :], 0.0).then_inc(s_ident, 1)
            pool.memset(eps_col[:, :], EPS_LN).then_inc(s_ident, 1)
            pool.memset(x1t[:, 0:1], 0.0).then_inc(s_ident, 1)
            pool.wait_ge(s_ident, 3)
            pool.affine_select(out=ident[:, :], in_=ident[:, :], compare_op=ALU.not_equal, fill=1.0,
                               base=0, pattern=[[-1, P]], channel_multiplier=1).then_inc(s_ident, 1)
            fill = pool.to_reg(MASKED)

            def project_lo(p, e, n):
                w, c = PROJECTIONS[n]
                whole = full[n % 2]
                if w < 2:
                    stage = (stage_q, stage_k)[w]
                    hi, lo = (stage[:, h, c * HALF:(c + 1) * HALF] for h in (0, 1))
                else:
                    hi, lo = (vs[:, e, 4 * c:4 * c + 4, :, h, :] for h in (0, 1))
                    whole = whole.rearrange("p (t a d) -> p t a d", t=4, a=2)
                pool.wait_ge(s_proj_full, NPROJ * p + n + 1)
                pool.tensor_tensor(lo, whole, hi.bitcast(F32), ALU.subtract).then_inc(s_proj_lo, 1)

            for n in range(NPROJ):
                project_lo(0, 0, n)

            def body(i, e, p, live):
                for k in range(SLOTS):
                    if live:
                        t = k % TILES
                        block_of = tile[:, k % RING, t * P:(t + 1) * P]
                        pool.wait_ge(s_evac, SLOTS * p + k + 1)
                        pool.sem_inc(s_pool_turn, 1)
                        pool.affine_select(out=block_of, in_=block_of, compare_op=ALU.is_ge, fill=fill, base=0,
                                           pattern=[[-1, P]], channel_multiplier=1).then_inc(s_masked, 1)
                    if k - 1 in PROJECT_AT and not last(p):
                        project_lo(p + 1, 1 - e, PROJECTION_OF_SLOT[k - 1])
                    if k in NORM_AT:
                        a, g, before = NORM_AT[k]
                        if (before and first(p)) or (not before and not live):
                            continue
                        q, par = (p - 1, 1 - e) if before else (p, e)
                        cols = ot[:, par, a, g * HALF:(g + 1) * HALF].rearrange("p (t i) -> p t i", t=4)
                        pool.wait_ge(s_rb, 16 * (2 * q + a + 1))
                        pool.wait_ge(s_ot, 4 * q + 2 * a + g + 1)
                        pool.sem_inc(s_pool_turn, 1)
                        pool.tensor_tensor(cols, cols,
                                           rb[:, a, :].rearrange("p (i t) -> p t i", t=TILES)[:, 4 * g:4 * g + 4, :],
                                           ALU.mult).then_inc(s_norm, 1)

            pairs_of(pool, body)

        @block.scalar
        def _(act):
            act.wait_ge(s_small, 48)
            for b in range(B):
                act.wait_ge(s_xturned, b + 1)
                if b >= 2:
                    act.wait_ge(s_xstored[b % 2], 16 * (b // 2))
                act.activation(x_part[:, b % 2, 0, :], ps_s[b % 2][:, :], ACT.Copy).then_inc(s_xhi, 1)
                act.activation(y[:, b * N:(b + 1) * N], ps_s[b % 2][:, :], ACT.Identity,
                               bias=bo_col[:, 0:1]).then_inc(s_xhi, 1)
            act.wait_ge(s_wraw, 32)
            for w in range(3):
                act.activation(w_hi[:, w * N:(w + 1) * N], w_raw[:, w * N:(w + 1) * N], ACT.Copy).then_inc(s_whi, 1)

            def project_hi(p, e, n):
                w, c = PROJECTIONS[n]
                bank = ps_x[BANK["project", n]]
                act.wait_ge(s_proj, NPROJ * p + n + 1)
                if w < 2:
                    if c == 0:
                        at_least(act, (s_qs, s_ks)[w], 64 * p)
                    dst, src = (stage_q, stage_k)[w][:, 0, c * HALF:(c + 1) * HALF], bank[:, :]
                else:
                    if c == 0:
                        at_least(act, s_pv, 4 * (p - 1))
                    dst = vs[:, e, 4 * c:4 * c + 4, :, 0, :]
                    src = bank[:, :].rearrange("p (t a d) -> p t a d", t=4, a=2)
                act.activation(dst, src, ACT.Copy).then_inc(s_proj_hi, 1)
                at_least(act, s_proj_lo, NPROJ * p + n - 1)
                act.activation(full[n % 2], bank[:, :], ACT.Copy).then_inc(s_proj_full, 1)

            for n in range(NPROJ):
                project_hi(0, 0, n)

            def exp_of(p, k):
                a, t = divmod(k, TILES)
                if t == 0:
                    at_least(act, s_eps, 2 * (p - 1) + a + 1)
                act.wait_ge(s_masked, SLOTS * p + k + 1)
                cols = tile[:, k % RING, 0:(t + 1) * P]
                act.activation(cols, cols, ACT.Exp, bias=neg_max[:, k % RING:k % RING + 1], scale=-1.0,
                               accum_out=sums[:, a, t:t + 1]).then_inc(s_exp, 1)

            def high_of(p, k):
                a, t = divmod(k, TILES)
                for q in range(FIRST_QUAD[t], FIRST_QUAD[t + 1]):
                    _, j, m = QUADS[q]
                    n = a * NQ + q
                    pt, g = (pt0, 0) if t < 4 else (pt1, 1)
                    if q in (0, FIRST_QUAD[4]):
                        at_least(act, s_pv, 4 * p + 2 * a + g - 1)
                    act.wait_ge(s_turned, 2 * NQ * p + n + 1)
                    act.activation(pt[:, 0, j:j + m, (t - 4 * g) * P:(t - 4 * g + 1) * P],
                                   ps_t[BANK["quad", n]][:, 0:m, :], ACT.Copy).then_inc(s_hi, 1)

            def take_values(p, e, a, g):
                if a == 0 and g == 0:
                    at_least(act, s_out, 2 * (p - 1))
                act.wait_ge(s_pv, 4 * p + 2 * a + g + 1)
                act.activation(ot[:, e, a, g * HALF:(g + 1) * HALF], ps_o[:, :], ACT.Copy).then_inc(s_ot, 1)

            def body(i, e, p, live):
                for k in range(SLOTS):
                    if k == 0 and not first(p):
                        exp_of(p - 1, SLOTS - 1)
                    if k >= 1 and live:
                        exp_of(p, k - 1)
                    if k - 1 in PROJECT_AT and not last(p):
                        project_hi(p + 1, 1 - e, PROJECTION_OF_SLOT[k - 1])
                    if k < TURN_LAG and not first(p):
                        high_of(p - 1, SLOTS - TURN_LAG + k)
                    if k >= TURN_LAG and live:
                        high_of(p, k - TURN_LAG)
                    if k in PV_AT:
                        a, g, js, before = PV_AT[k]
                        if js[-1] == 4 * g + 3 and not (before and first(p)) and (before or live):
                            q, par = (p - 1, 1 - e) if before else (p, e)
                            take_values(q, par, a, g)

            pairs_of(act, body)

            act.wait_ge(f_wt, 1)
            act.activation(ffn_t[:, :, :], ps_t[0][:, 0:3, :], ACT.Copy).then_inc(f_wc, 1)

            def deviations(b, half):
                act.wait_ge(f_mv, TILES * norms_before(b, half) + TILES)
                act.activation(dev[half][:, :], mv[half][:, :, 1], ACT.Sqrt, bias=eps_col[:, 0:1]).then_inc(f_dev, 1)

            for b in range(B + 1):
                if b < B:
                    deviations(b, 0)
                if b > 0:
                    for c in range(2):
                        act.wait_ge(f_k, 2 * (b - 1) + c + 1)
                        act.activation(relu[(b - 1) % 2][:, c * HALF:(c + 1) * HALF], ps_x[c][:, :], ACT.Relu
                                       ).then_inc(f_relu, 1)
                if b < B:
                    act.wait_ge(f_x1t, b + 1)
                    at_least(act, f_mix, 2 * b)
                    act.activation(x1t[:, 1:N + 1], ps_s[1][:, :], ACT.Copy).then_inc(f_x1c, 1)
                    act.wait_ge(f_x1c, b + 1)
                    at_least(act, f_r, 2 * (b - 1))
                    for n, mix in enumerate((mix_r, mix_k)):
                        act.activation(mix[b % 2], x1t[:, 0:N], ACT.Copy, scale=small[:, 2 + n:3 + n]
                                       ).then_inc(f_prev, 1)
                if b > 0:
                    for c, bank in enumerate((ps_x[2], ps_o)):
                        act.wait_ge(f_r, 2 * (b - 1) + c + 1)
                        act.activation(gate[(b - 1) % 2][:, 4 * c:4 * c + 4, :],
                                       bank[:, :].rearrange("p (t c) -> p t c", t=4), ACT.Sigmoid).then_inc(f_sig, 1)
                    deviations(b - 1, 1)

        @block.vector
        def _(dve):
            dve.wait_ge(s_small, 48)
            dve.tensor_scalar(small[:, 2:4], small[:, 0:2], -1.0, 1.0, ALU.mult, ALU.add)
            for b in range(B):
                dve.wait_ge(s_xhi, 2 * b + 2)
                dve.tensor_tensor(x_part[:, b % 2, 1, :], ps_s[b % 2][:, :], x_part[:, b % 2, 0, :].bitcast(F32),
                                  ALU.subtract).then_inc(s_xlo, 1)
            for w in range(3):
                dve.wait_ge(s_whi, w + 1)
                dve.tensor_tensor(w_lo[:, w * N:(w + 1) * N], w_raw[:, w * N:(w + 1) * N],
                                  w_hi[:, w * N:(w + 1) * N].bitcast(F32), ALU.subtract).then_inc(s_wlo, 1)

            def evacuate(p, k):
                if k >= RING:
                    a, t = divmod(k - RING, TILES)
                    dve.wait_ge(s_turned, 2 * NQ * p + a * NQ + FIRST_QUAD[t + 1])
                else:
                    a, t = divmod(SLOTS + k - RING, TILES)
                    at_least(dve, s_turned, 2 * NQ * (p - 1) + a * NQ + FIRST_QUAD[t + 1])
                dve.wait_ge(s_scores, SLOTS * p + k + 1)
                dve.tensor_scalar(tile[:, k % RING, :], ps_s[k % 2][:, :], -SCALE, None, ALU.mult, ALU.min,
                                  accum_out=neg_max[:, k % RING:k % RING + 1]).then_inc(s_evac, 1)

            def low_of(p, k):
                a, t = divmod(k, TILES)
                for q in range(FIRST_QUAD[t], FIRST_QUAD[t + 1]):
                    _, j, m = QUADS[q]
                    n = a * NQ + q
                    pt, g = (pt0, 0) if t < 4 else (pt1, 1)
                    hi, lo = (pt[:, h, j:j + m, (t - 4 * g) * P:(t - 4 * g + 1) * P] for h in (0, 1))
                    dve.wait_ge(s_hi, 2 * NQ * p + n + 1)
                    dve.tensor_tensor(lo, ps_t[BANK["quad", n]][:, 0:m, :], hi.bitcast(F32), ALU.subtract
                                      ).then_inc(s_lo, 1)

            def recips_of(p, a):
                dve.wait_ge(s_exp, SLOTS * p + TILES * (a + 1))
                dve.tensor_scalar(sums_eps[:, a, :], sums[:, a, :], EPS_SUM, None, ALU.add).then_inc(s_eps, 1)
                at_least(dve, s_rdram, 16 * (2 * (p - 1) + a + 1))
                dve.wait_ge(s_eps, 2 * p + a + 1)
                dve.reciprocal(recips[:, a, :], sums_eps[:, a, :]).then_inc(s_recip, 1)

            def add_out(i, e, p, c):
                q = p - 1
                b = q // PAIRS if isinstance(q, int) else ((i - 1) // 4 if e == 0 else i // 4)
                cols = y[:, bass.ds(b * N + c * HALF, HALF)]
                dve.wait_ge(s_out, 2 * q + c + 1)
                dve.tensor_tensor(cols, cols, ps_x[BANK["out", c]][:, :], ALU.add).then_inc(s_yadd, 1)

            def body(i, e, p, live):
                for k in range(SLOTS):
                    if live:
                        evacuate(p, k)
                    if k == 1 and not first(p):
                        recips_of(p - 1, 1)
                    if k == 9 and live:
                        recips_of(p, 0)
                    if k - 1 in OUT_AT and not first(p):
                        add_out(i, e, p, OUT_AT[k - 1])
                    if k < TURN_LAG and not first(p):
                        low_of(p - 1, SLOTS - TURN_LAG + k)
                    if k >= TURN_LAG and live:
                        low_of(p, k - TURN_LAG)

            pairs_of(dve, body)

            def moments(b, half, src):
                done = TILES * norms_before(b, half)
                for t in range(TILES):
                    dve.bn_stats(stats[:, t, :], src[:, t, :]).then_inc(f_stats, 1)
                for t in range(TILES):
                    dve.wait_ge(f_stats, done + t + 1)
                    dve.bn_aggr(mv[half][:, t, :], stats[:, t, :]).then_inc(f_mv, 1)

            def normed(b, half, dst, src, done):
                n = norms_before(b, half) + 1
                dve.wait_ge(f_dev, n)
                dve.reciprocal(rstd[half][:, :], dev[half][:, :]).then_inc(f_rstd, 1)
                dve.wait_ge(f_rstd, n)
                for t in range(TILES):
                    ins = dve.tensor_scalar(dst[:, t, :], src[:, t, :], mv[half][:, t, 0:1], rstd[half][:, t:t + 1],
                                            ALU.subtract, ALU.mult)
                ins.then_inc(done, 1)

            for b in range(B + 1):
                q = (b - 1) % 2
                if b < B:
                    dve.wait_ge(f_yt, b + 1)
                    moments(b, 0, tokens(ps_s[0][:, :]))
                if b > 0:
                    for c in range(2):
                        dve.wait_ge(f_relu, 2 * (b - 1) + c + 1)
                        cols = relu[q][:, c * HALF:(c + 1) * HALF]
                        dve.scalar_tensor_tensor(out=cols, in0=ps_x[c][:, :], scalar=0.0, in1=cols,
                                                 op0=ALU.max, op1=ALU.mult).then_inc(f_act, 1)
                if b < B:
                    normed(b, 0, x1[b % 2], tokens(ps_s[0][:, :]), f_x1)
                if b > 0:
                    for c in range(2):
                        dve.wait_ge(f_sig, 2 * (b - 1) + c + 1)
                        dve.wait_ge(f_v, 2 * (b - 1) + c + 1)
                        part = gate[q][:, 4 * c:4 * c + 4, :]
                        dve.tensor_tensor(part, part, ps_x[c][:, :].rearrange("p (t c) -> p t c", t=4), ALU.mult
                                          ).then_inc(f_gate, 1)
                    dve.wait_ge(f_gate, 2 * b)
                    dve.tensor_tensor(gate[q], gate[q], x1[q], ALU.add).then_inc(f_sum, 1)
                    dve.wait_ge(f_sum, b)
                    moments(b - 1, 1, gate[q])
                if b < B:
                    for n, mix in enumerate((mix_r, mix_k)):
                        dve.wait_ge(f_prev, 2 * b + n + 1)
                        dve.scalar_tensor_tensor(out=mix[b % 2], in0=x1t[:, 1:N + 1], scalar=small[:, n:n + 1],
                                                 in1=mix[b % 2], op0=ALU.mult, op1=ALU.add).then_inc(f_mix, 1)
                if b > 0:
                    normed(b - 1, 1, fin[b - 1], gate[q], f_fin)

        @block.tensor
        def _(pe):
            mm = nc.tensor.matmul
            turn = nc.tensor.transpose
            pe.wait_ge(s_ident, 4)
            for b in range(B):
                if b == 0:
                    pe.wait_ge(s_xraw, 16 * B)
                if b >= 2:
                    pe.wait_ge(s_xlo, b - 1)
                for t in range(TILES):
                    ins = turn(ps_s[b % 2][:, t * P:(t + 1) * P], tile[:, b, t * P:(t + 1) * P], ident[:, :])
                ins.then_inc(s_xturned, 1)

            def drained(p, kind, n):
                at = next(m for m, u in enumerate(SHARED) if (u[0], u[2]) == (kind, n))
                for back in range(at - 1, at - 1 - 2 * len(SHARED), -1):
                    q, m = (p, back) if back >= 0 else (p - 1, back + len(SHARED))
                    what, k, u = SHARED[m]
                    if m % NSHARED != at % NSHARED or back < -len(SHARED):
                        continue
                    if isinstance(q, int):
                        owner = {"quad": q - (k < TURN_LAG), "project": q + 1, "out": q - 1}[what]
                        if q < 0 or not 0 <= owner < ALL_PAIRS:
                            continue
                    if what == "quad":
                        pe.wait_ge(s_lo, 2 * NQ * (q - (k < TURN_LAG)) + u + 1)
                    elif what == "project":
                        pe.wait_ge(s_proj_full, NPROJ * (q + 1) + u + 1)
                    else:
                        pe.wait_ge(s_yadd, 2 * (q - 1) + u + 1)
                    return

            def project(n):
                bank = ps_x[BANK["project", n]]
                w, c = PROJECTIONS[n]
                parts = ((0, 0), (1, 0), (0, 1))
                if w < 2:
                    for m, (wh, xh) in enumerate(parts):
                        ins = mm(bank[:, :], ws[:, w, wh, :], xs[:, xh, c * HALF:(c + 1) * HALF],
                                 start=(m == 0), stop=(m == 2))
                else:
                    for t in range(4):
                        for m, (wh, xh) in enumerate(parts):
                            ins = mm(bank[:, t * P:(t + 1) * P], xs[:, xh, (4 * c + t) * P:(4 * c + t + 1) * P],
                                     ws[:, w, wh, :], start=(m == 0), stop=(m == 2))
                ins.then_inc(s_proj, 1)

            pe.wait_ge(s_ws, 16)
            pe.wait_ge(s_xs, 16)
            for n in range(NPROJ):
                for m in range(n):
                    if BANK["project", m] == BANK["project", n]:
                        at_least(pe, s_proj_full, m + 1)
                project(n)
            pe.wait_ge(s_proj_full, NPROJ)

            def scores(p, e, k):
                a, t = divmod(k, TILES)
                if k == 0:
                    pe.wait_ge(s_qs, 64 * (p + 1))
                    pe.wait_ge(s_ks, 64 * (p + 1))
                if k < 2 and first(p):
                    pe.wait_ge(s_xlo, B)
                at_least(pe, s_evac, SLOTS * p + k - 1)
                q = qs[:, e, a, t * P:(t + 1) * P]
                for c in range(2):
                    for h in range(2):
                        ins = mm(ps_s[k % 2][:, c * HALF:(c + 1) * HALF], q, ks[:, e, a, h, c * HALF:(c + 1) * HALF],
                                 start=(h == 0), stop=(h == 1))
                ins.then_inc(s_scores, 1)

            def turn_tile(p, k):
                a, t = divmod(k, TILES)
                pe.wait_ge(s_exp, SLOTS * p + k + 1)
                for q in range(FIRST_QUAD[t], FIRST_QUAD[t + 1]):
                    _, j, m = QUADS[q]
                    n = a * NQ + q
                    drained(p + (1 if k + TURN_LAG >= SLOTS else 0), "quad", n)
                    for b in range(m):
                        ins = turn(ps_t[BANK["quad", n]][:, b, :], tile[:, k % RING, (j + b) * P:(j + b + 1) * P],
                                   ident[:, :])
                    ins.then_inc(s_turned, 1)

            def values(p, e, a, g, js):
                pt = (pt0, pt1)[g]
                if js[0] == 0:
                    pe.wait_ge(s_proj_lo, NPROJ * (p + 1))
                    pe.wait_ge(s_lo, 2 * NQ * p + a * NQ + FIRST_QUAD[4 * g + 4])
                    at_least(pe, s_ot, 4 * p + 2 * a + g)
                final = 4 * g + 3
                for j in js:
                    off = max(j - 4 * g, 0) * P
                    for h in range(2):
                        ins = mm(ps_o[:, off:HALF], vs[:, e, j, a, :, :].rearrange("p h d -> p (h d)"),
                                 pt[:, h, j, off:HALF], start=(j == 0 and h == 0), stop=(j == final and h == 1))
                if js[-1] == final:
                    ins.then_inc(s_pv, 1)

            def project_out(p, e, c):
                if c == 0:
                    pe.wait_ge(s_norm, 4 * (p + 1))
                    pe.wait_ge(s_wo, 32 * (p + 1))
                for a in range(2):
                    ins = mm(ps_x[BANK["out", c]][:, :], wos[:, a, :], ot[:, e, a, c * HALF:(c + 1) * HALF],
                             start=(a == 0), stop=(a == 1))
                ins.then_inc(s_out, 1)

            def body(i, e, p, live):
                for k in range(SLOTS):
                    if live:
                        scores(p, e, k)
                    if k in PV_AT:
                        a, g, js, before = PV_AT[k]
                        if before and not first(p):
                            values(p - 1, 1 - e, a, g, js)
                        if not before and live:
                            values(p, e, a, g, js)
                    if k < TURN_LAG and not first(p):
                        turn_tile(p - 1, SLOTS - TURN_LAG + k)
                    if k >= TURN_LAG and live:
                        turn_tile(p, k - TURN_LAG)
                    if k in PROJECT_AT and not last(p):
                        n = PROJECTION_OF_SLOT[k]
                        if n == 0:
                            pe.wait_ge(s_ws, 16 * (p + 2))
                            if e == 1:
                                pe.wait_ge(s_xs, 16 * (i + 2))
                        drained(p, "project", n)
                        project(n)
                    if k in OUT_AT and not first(p):
                        c = OUT_AT[k]
                        drained(p, "out", c)
                        project_out(p - 1, 1 - e, c)

            pairs_of(pe, body)

            pe.wait_ge(f_w, 48)
            pe.wait_ge(s_lo, 2 * NQ * ALL_PAIRS)
            pe.wait_ge(s_yadd, 2 * ALL_PAIRS)
            for n in range(3):
                ins = turn(ps_t[0][:, n, :], w_ffn[:, n, :], ident[:, :])
            ins.then_inc(f_wt, 1)
            pe.wait_ge(s_evac, SLOTS * ALL_PAIRS)
            pe.wait_ge(s_ot, 4 * ALL_PAIRS)
            for b in range(B + 1):
                q = (b - 1) % 2
                if b < B:
                    at_least(pe, f_x1, b)
                    for t in range(TILES):
                        ins = turn(ps_s[0][:, t * P:(t + 1) * P], y[:, b * N + t * P:b * N + (t + 1) * P],
                                   ident[:, :])
                    ins.then_inc(f_yt, 1)
                if b > 0:
                    pe.wait_ge(f_wc, 1)
                    pe.wait_ge(f_mix, 2 * b)
                    at_least(pe, f_gate, 2 * (b - 1))
                    for c in range(2):
                        mm(ps_x[c][:, :], ffn_t[:, 1, :], mix_k[q][:, c * HALF:(c + 1) * HALF], start=True, stop=True
                           ).then_inc(f_k, 1)
                    at_least(pe, f_sig, 2 * (b - 1))
                    for c, bank in enumerate((ps_x[2], ps_o)):
                        for t in range(4):
                            ins = mm(bank[:, t * P:(t + 1) * P], mix_r[q][:, (4 * c + t) * P:(4 * c + t + 1) * P],
                                     ffn_t[:, 0, :], start=True, stop=True)
                        ins.then_inc(f_r, 1)
                if b < B:
                    pe.wait_ge(f_x1, b + 1)
                    at_least(pe, f_x1c, b)
                    for t in range(TILES):
                        ins = turn(ps_s[1][:, t * P:(t + 1) * P], x1[b % 2][:, t, :], ident[:, :])
                    ins.then_inc(f_x1t, 1)
                if b > 0:
                    for c in range(2):
                        pe.wait_ge(f_act, 2 * (b - 1) + c + 1)
                        for t in range(4):
                            ins = mm(ps_x[c][:, t * P:(t + 1) * P], relu[q][:, (4 * c + t) * P:(4 * c + t + 1) * P],
                                     ffn_t[:, 2, :], start=True, stop=True)
                        ins.then_inc(f_v, 1)


_INS = ["L0_attn_x", "L0_attn_Wq", "L0_attn_Wkv", "L0_attn_Wo", "L0_attn_bo",
        "L0_ffn_W_r", "L0_ffn_W_k", "L0_ffn_W_v", "L0_ffn_mu_r", "L0_ffn_mu_k"]


def kernel(**inputs):
    import numpy as np
    import concourse.bacc as bacc
    from concourse.bass_utils import run_bass_kernel_spmd

    nc = bacc.Bacc("TRN2", target_bir_lowering=False, num_devices=1)
    arrays, args = {}, []
    for name in _INS:
        a = np.ascontiguousarray(inputs[name])
        arrays[f"in_{name}"] = a
        args.append(nc.dram_tensor(f"in_{name}", a.shape, mybir.dt.from_np(a.dtype), kind="ExternalInput").ap())
    out = nc.dram_tensor("out", (B, N, C), F32, kind="ExternalOutput").ap()
    build(nc, *args, out)
    return run_bass_kernel_spmd(nc, [arrays], core_ids=[0]).results[0]["out"]
```

```python
from contextlib import ExitStack

import concourse.bass as bass
from concourse import mybir

F32 = mybir.dt.float32
F32R = mybir.dt.float32r
ALU = mybir.AluOpType
ACT = mybir.ActivationFunctionType

P = 128
B, N, C = 4, 1024, 128
HEADS, DH = 16, 64
TILES = N // P
PAIRS = HEADS // 2
ALL_PAIRS = B * PAIRS
SLOTS = 2 * TILES
HALF = N // 2
SCALE = DH ** -0.5
EPS_SUM = 1e-8
EPS_LN = 1e-5
TURN_LAG = 3
RING = 4
MASKED = 3.0e38

FIRST_BLOCKS = [t + 1 if t < 4 else (t + 1) // 2 for t in range(TILES)]
QUADS = [(t, j, m) for t, h in enumerate(FIRST_BLOCKS) for j, m in ((0, h), (h, t + 1 - h)) if m]
NQ = len(QUADS)
FIRST_QUAD = [next(n for n, q in enumerate(QUADS) if q[0] == t) for t in range(TILES)] + [NQ]

PV_AT = {
    8: (0, 0, (0,), False),
    9: (0, 0, (1, 2), False),
    10: (0, 0, (3,), False),
    12: (0, 1, (0, 1, 2), False),
    13: (0, 1, (3, 4), False),
    14: (0, 1, (5, 6, 7), False),
    0: (1, 0, (0, 1), True),
    1: (1, 0, (2,), True),
    2: (1, 0, (3,), True),
    5: (1, 1, (0, 1), True),
    6: (1, 1, (2, 3, 4, 5, 6, 7), True),
}
PROJECTIONS = [("q", 0), ("q", 1), ("k", 0), ("k", 1), ("v", 0), ("v", 1), ("v", 2), ("v", 3)]
PROJECT_AT = [{0: 0, 1: 1, 2: 2, 4: 3, 5: 4, 6: 5, 8: 6, 10: 7}, {2: 0, 4: 1, 8: 2, 9: 3}]
NQK = 4
OUT_AT = {13: 0, 15: 1}
JOIN_AT = {8: 0, 12: 1}
NORM_AT = {9: 0, 13: 1}


def norms_before(b, half):
    return max(2 * b - 1, 0) if half == 0 else min(2 * b + 2, 2 * B - 1)


def at_least(eng, sem, value):
    if isinstance(value, int) and value <= 0:
        return
    eng.wait_ge(sem, value)


NORM_AHEAD = 3
MIX_AHEAD = 7

NSHARED = 3
SHARED = [[], []]
for _e in range(2):
    for _k in range(SLOTS):
        _a, _t = divmod((_k - TURN_LAG) % SLOTS, TILES)
        SHARED[_e] += [("quad", _k, _a * NQ + _q) for _q in range(FIRST_QUAD[_t], FIRST_QUAD[_t + 1])]
        if _k in PROJECT_AT[_e]:
            SHARED[_e].append(("project", _k, PROJECT_AT[_e][_k]))
        if _k in OUT_AT:
            SHARED[_e].append(("out", _k, OUT_AT[_k]))
BANK = [{(kind, n): at % NSHARED for at, (kind, _, n) in enumerate(units)} for units in SHARED]


def projected(p, e):
    return 6 * p + (4 if e == 0 else 6)


def build(nc, x, wq, wkv, wo, bo, w_r, w_k, w_v, mu_r, mu_k, out):
    x_dram = nc.dram_tensor("x_split", [B, P, 2, N], F32).ap()
    wqk_dram = nc.dram_tensor("wqk_split", [PAIRS, P, 2, 2, P], F32).ap()
    wv_dram = nc.dram_tensor("wv_split", [PAIRS // 2, P, 2, 2 * P], F32).ap()
    r_dram = nc.dram_tensor("recips", [2, N], F32).ap()

    with ExitStack() as ctx:
        def sb(name, shape, dt=F32):
            return ctx.enter_context(nc.sbuf_tensor(name, shape, dt))

        def psum(name, shape):
            return ctx.enter_context(nc.psum_tensor(name, shape, F32))

        def sem(name):
            return ctx.enter_context(nc.semaphore(name))

        ident = sb("ident", [P, P])
        xs = sb("xs", [P, 2, N], F32R)
        ws = sb("ws", [P, 2, 2, P], F32R)
        wv = sb("wv", [P, 2, 2 * P], F32R)
        wos = sb("wos", [P, P])
        stage_q = sb("stage_q", [P, 2, N], F32R)
        stage_k = sb("stage_k", [P, 2, N], F32R)
        qs = sb("qs", [P, 2, 2, N], F32R)
        ks = sb("ks", [P, 2, 2, 2, N], F32R)
        vs = sb("vs", [P, TILES, 2, 2, 2, DH], F32R)
        vs_heads = vs[:, :, :, :, :, :].rearrange("p t e a h d -> p (t e a) h d")
        tile = sb("tile", [P, RING, N])
        neg_max = sb("neg_max", [P, RING])
        sums = sb("sums", [P, 2, TILES])
        sums_eps = sb("sums_eps", [P, 2, TILES])
        recips = sb("recips_sb", [P, 2, TILES])
        pt0 = sb("pt0", [P, 2, 4, HALF], F32R)
        pt1 = sb("pt1", [P, 2, 8, HALF], F32R)
        ot = sb("ot", [P, 2, N])
        ot_lo = sb("ot_lo", [P, N])
        rb = sb("rb", [P, N])
        y = sb("y", [P, B * N])
        spare = sb("spare", [P, 2, N])
        x1t = sb("x1t", [P, 1 + N])
        full = [x1t[:, 1:1 + HALF], x1t[:, 1 + HALF:1 + N]]
        bo_col = sb("bo_col", [P, 1])
        small = sb("small", [P, 4])
        eps_col = sb("eps_col", [P, 1])
        ffn_t = sb("ffn_t", [P, 3, C])
        stats = sb("stats", [P, TILES, 6])
        mv = [sb(f"mv{n}", [P, TILES, 2]) for n in range(2)]
        dev = [sb(f"dev{n}", [P, TILES]) for n in range(2)]
        rstd = [sb(f"rstd{n}", [P, TILES]) for n in range(2)]

        ps_s = [psum("ps_s0", [P, N]), psum("ps_s1", [P, N])]
        ps_x = [psum(f"ps_x{n}", [P, HALF]) for n in range(NSHARED)]
        ps_t = [bank[:, :].rearrange("p (b i) -> p b i", b=4) for bank in ps_x]
        ps_o = psum("ps_o", [P, HALF])

        w_raw = [ot[:, 0, :], ot[:, 1, :], ot_lo[:, :]]
        w_first = rb[:, 0:4 * P]
        idle_pt = pt1[:, :, :, :].rearrange("p h j n -> p (h j n)")
        w_hi = idle_pt[:, 0:3 * N]
        w_lo = idle_pt[:, 3 * N:6 * N]
        x_part = [xs[:, :, :],
                  vs[:, TILES // 2:TILES, :, :, :, :].rearrange("p (h t) e a i d -> p h (t e a i d)", h=2),
                  idle_pt[:, 6 * N:8 * N].rearrange("p (h n) -> p h n", h=2),
                  qs[:, 1, :, :]]

        s_ident = sem("s_ident")
        s_xraw = sem("s_xraw")
        s_x0raw = sem("s_x0raw")
        s_wraw = sem("s_wraw")
        s_w0raw = sem("s_w0raw")
        s_w0hi = sem("s_w0hi")
        s_w0lo = sem("s_w0lo")
        s_small = sem("s_small")
        s_xturned = sem("s_xturned")
        s_xhi = sem("s_xhi")
        s_xlo = sem("s_xlo")
        s_xstored = sem("s_xstored")
        s_whi = sem("s_whi")
        s_wlo = sem("s_wlo")
        s_wstored = sem("s_wstored")
        s_xs = sem("s_xs")
        s_ws = sem("s_ws")
        s_wv = sem("s_wv")
        s_wo = sem("s_wo")
        s_proj = sem("s_proj")
        s_proj_full = sem("s_proj_full")
        s_proj_lo = sem("s_proj_lo")
        s_qs = sem("s_qs")
        s_ks = sem("s_ks")
        s_scores = sem("s_scores")
        s_evac = sem("s_evac")
        s_masked = sem("s_masked")
        s_exp = sem("s_exp")
        s_turned = sem("s_turned")
        s_hi = sem("s_hi")
        s_lo = sem("s_lo")
        s_pv = sem("s_pv")
        s_ot = sem("s_ot")
        s_eps = sem("s_eps")
        s_recip = sem("s_recip")
        s_rdram = sem("s_rdram")
        s_rb = sem("s_rb")
        s_join = sem("s_join")
        s_norm = sem("s_norm")
        s_out = sem("s_out")
        s_yadd = sem("s_yadd")
        s_pool_turn = sem("s_pool_turn")
        s_sp_turn = sem("s_sp_turn")
        f_yt = sem("f_yt")
        f_stats = sem("f_stats")
        f_mv = sem("f_mv")
        f_dev = sem("f_dev")
        f_rstd = sem("f_rstd")
        f_x1 = sem("f_x1")
        f_x1t = sem("f_x1t")
        f_x1c = sem("f_x1c")
        f_prev = sem("f_prev")
        f_mix = sem("f_mix")
        f_k = sem("f_k")
        f_relu = sem("f_relu")
        f_act = sem("f_act")
        f_r = sem("f_r")
        f_sig = sem("f_sig")
        f_v = sem("f_v")
        f_gate = sem("f_gate")
        f_sum = sem("f_sum")
        f_fin = sem("f_fin")
        f_w = sem("f_w")
        f_wt = sem("f_wt")
        f_wc = sem("f_wc")
        f_stored = sem("f_stored")

        def tokens(cols):
            return cols.rearrange("p (t c) -> p t c", t=TILES)

        x1 = [tokens(tile[:, n, :]) for n in (0, 1)]
        gate = [tokens(tile[:, n, :]) for n in (2, 3)]
        mix_r = [ot[:, n, :] for n in (0, 1)]
        mix_k = [spare[:, n, :] for n in (0, 1)]
        relu = [ot_lo[:, :], rb[:, :]]
        fin = [tokens(y[:, b * N:(b + 1) * N]) for b in range(B)]
        w_ffn = spare[:, 0, 0:3 * C].rearrange("p (w c) -> p w c", w=3)

        block = ctx.enter_context(nc.Block())

        def pairs_of(eng, body):
            body(0, 0, 0, True)
            body(0, 1, 1, True)
            with eng.Fori(1, ALL_PAIRS // 2 - 1) as i:
                body(i, 0, 2 * i, True)
                body(i, 1, 2 * i + 1, True)
            body(ALL_PAIRS // 2 - 1, 0, ALL_PAIRS - 2, True)
            body(ALL_PAIRS // 2 - 1, 1, ALL_PAIRS - 1, True)
            body(ALL_PAIRS // 2, 0, ALL_PAIRS, False)

        def last(p):
            return isinstance(p, int) and p >= ALL_PAIRS - 1

        def first(p):
            return isinstance(p, int) and p == 0

        @block.sync
        def _(sp):
            def load_tokens(b, done):
                sp.dma_start(tile[:, b, :].rearrange("p (t c) -> p t c", t=TILES),
                             x[b, :, :].rearrange("(t p) c -> p t c", p=P)).then_inc(done, 16)

            load_tokens(0, s_x0raw)
            sp.dma_start(w_first[:, 0:P], wq[:, 0:P]).then_inc(s_w0raw, 16)
            sp.dma_start(w_first[:, P:2 * P], wkv[:, 0:P]).then_inc(s_w0raw, 16)
            sp.dma_start(w_first[:, 2 * P:4 * P], wkv[:, N:N + 2 * P]).then_inc(s_w0raw, 16)
            sp.dma_start(w_raw[0], wq).then_inc(s_wraw, 16)
            sp.dma_start(w_raw[1], wkv[:, 0:N]).then_inc(s_wraw, 16)
            sp.dma_start(w_raw[2], wkv[:, N:2 * N]).then_inc(s_wraw, 16)
            sp.dma_start(bo_col[:, :], bo.rearrange("(p a) -> p a", a=1)).then_inc(s_small, 16)
            for b in range(1, B):
                load_tokens(b, s_xraw)
            sp.dma_start(small[:, 0:1], mu_r.rearrange("(p a) -> p a", a=1)).then_inc(s_small, 16)
            sp.dma_start(small[:, 1:2], mu_k.rearrange("(p a) -> p a", a=1)).then_inc(s_small, 16)
            for n, w in enumerate((w_r, w_k, w_v)):
                sp.dma_start(w_ffn[:, n, :], w).then_inc(f_w, 16)

            def load_weights(p):
                src = wqk_dram[bass.ds(p % PAIRS, 1), :, :, :, :].rearrange("a p w h n -> (a p) w h n")
                sp.dma_start(ws[:, :, :, :].bitcast(F32), src).then_inc(s_ws, 16)

            def load_v_weights(i):
                src = wv_dram[bass.ds(i % (PAIRS // 2), 1), :, :, :].rearrange("a p h n -> (a p) h n")
                sp.dma_start(wv[:, :, :].bitcast(F32), src).then_inc(s_wv, 16)

            def load_x(i):
                b = i // 4
                src = x_dram[bass.ds(b, 1), :, :, :].rearrange("a p h n -> (a p) h n")
                sp.dma_start(xs[:, :, :].bitcast(F32), src).then_inc(s_xs, 16)

            def load_wo(p):
                sp.dma_start(wos[:, :], wo[bass.ds((p % PAIRS) * P, P), :]).then_inc(s_wo, 16)

            def stack_q(done, e):
                sp.wait_ge(s_proj_lo, done + 2)
                for a in range(2):
                    for h in range(2):
                        sp.dma_start(qs[h * DH:(h + 1) * DH, e, a, :].bitcast(F32),
                                     stage_q[a * DH:(a + 1) * DH, h, :].bitcast(F32)).then_inc(s_qs, 16)

            def stack_k(done, e):
                sp.wait_ge(s_proj_lo, done + 4)
                for a in range(2):
                    for h in range(2):
                        sp.dma_start(ks[h * DH:(h + 1) * DH, e, a, :, :].bitcast(F32),
                                     stage_k[a * DH:(a + 1) * DH, :, :].bitcast(F32)).then_inc(s_ks, 16)

            def spread_recips(p, a):
                n = 2 * p + a
                sp.wait_ge(s_recip, n + 1)
                at_least(sp, s_norm, 2 * p)
                sp.sem_inc(s_sp_turn, 1)
                sp.dma_start(r_dram[a, :].rearrange("(p t) -> p t", p=P), recips[:, a, :]).then_inc(s_rdram, 16)
                sp.wait_ge(s_rdram, 16 * (n + 1))
                sp.sem_inc(s_sp_turn, 1)
                sp.dma_start(rb[a * DH:(a + 1) * DH, :], r_dram[a, :].partition_broadcast(DH)).then_inc(s_rb, 16)

            load_wo(0)
            sp.wait_ge(s_xlo, 1)
            sp.dma_start(x_dram[0], x_part[0].bitcast(F32)).then_inc(s_xstored, 16)
            stack_q(0, 0)
            stack_k(0, 0)
            for w in range(3):
                sp.wait_ge(s_wlo, w + 1)
                for h, part in enumerate((w_hi, w_lo)):
                    cols = part[:, w * N:(w + 1) * N].bitcast(F32)
                    if w < 2:
                        dst = wqk_dram[:, :, w, h, :].rearrange("a p n -> p a n")
                        sp.dma_start(dst, cols.rearrange("p (a n) -> p a n", a=PAIRS)).then_inc(s_wstored, 16)
                    else:
                        dst = wv_dram[:, :, h, :].rearrange("a p n -> p a n")
                        sp.dma_start(dst, cols.rearrange("p (a n) -> p a n", a=PAIRS // 2)).then_inc(s_wstored, 16)
            for b in range(1, B):
                sp.wait_ge(s_xlo, b + 1)
                sp.dma_start(x_dram[b], x_part[b].bitcast(F32)).then_inc(s_xstored, 16)
            sp.wait_ge(s_xstored, 16 * B)
            sp.wait_ge(s_wstored, 16 * 6)

            def body(i, e, p, live):
                if not first(p):
                    spread_recips(p - 1, 1)
                if not last(p):
                    at_least(sp, s_scores, SLOTS * p)
                    sp.sem_inc(s_sp_turn, 1)
                    stack_q(projected(p, e), 1 - e)
                    stack_k(projected(p, e), 1 - e)
                if live:
                    spread_recips(p, 0)
                if not last(p) and not (isinstance(p, int) and p == ALL_PAIRS - 2):
                    sp.wait_ge(s_proj, projected(p, e) + len(PROJECT_AT[e]))
                    sp.sem_inc(s_sp_turn, 1)
                    load_weights(p + 2)
                    if e == 0:
                        load_v_weights(i + 1)
                        load_x(i + 1)
                if live and not first(p):
                    sp.wait_ge(s_out, 2 * p)
                    sp.sem_inc(s_sp_turn, 1)
                    load_wo(p)

            pairs_of(sp, body)

            for b in range(B):
                sp.wait_ge(f_fin, b + 1)
                sp.dma_start(out[b, :, :].rearrange("(t p) c -> p t c", p=P), fin[b]).then_inc(f_stored, 16)
            sp.wait_ge(f_stored, 16 * B)

        @block.gpsimd
        def _(pool):
            pool.memset(ident[:, :], 0.0).then_inc(s_ident, 1)
            pool.memset(eps_col[:, :], EPS_LN).then_inc(s_ident, 1)
            pool.memset(x1t[:, 0:1], 0.0).then_inc(s_ident, 1)
            pool.wait_ge(s_ident, 3)
            pool.affine_select(out=ident[:, :], in_=ident[:, :], compare_op=ALU.not_equal, fill=1.0,
                               base=0, pattern=[[-1, P]], channel_multiplier=1).then_inc(s_ident, 1)
            fill = pool.to_reg(MASKED)

            def project_lo(done, n):
                what, c = PROJECTIONS[n]
                whole = full[n % 2]
                if what == "v":
                    hi, lo = (vs_heads[:, 8 * c:8 * c + 8, h, :] for h in (0, 1))
                    whole = whole.rearrange("p (x d) -> p x d", d=DH)
                else:
                    stage = stage_q if what == "q" else stage_k
                    hi, lo = (stage[:, h, c * HALF:(c + 1) * HALF] for h in (0, 1))
                pool.wait_ge(s_proj_full, done + n + 1)
                pool.tensor_tensor(lo, whole, hi.bitcast(F32), ALU.subtract).then_inc(s_proj_lo, 1)

            for n in range(NQK):
                project_lo(0, n)

            def body(i, e, p, live):
                for k in range(SLOTS):
                    if live:
                        t = k % TILES
                        block_of = tile[:, k % RING, t * P:(t + 1) * P]
                        pool.wait_ge(s_evac, SLOTS * p + k + 1)
                        pool.sem_inc(s_pool_turn, 1)
                        pool.affine_select(out=block_of, in_=block_of, compare_op=ALU.is_ge, fill=fill, base=0,
                                           pattern=[[-1, P]], channel_multiplier=1).then_inc(s_masked, 1)
                    if live and k - 1 in PROJECT_AT[e]:
                        n = PROJECT_AT[e][k - 1]
                        if not (last(p) and n < NQK):
                            project_lo(projected(p, e), n)
                    if k in JOIN_AT and not first(p):
                        c = JOIN_AT[k]
                        cols = slice(c * HALF, (c + 1) * HALF)
                        pool.wait_ge(s_ot, 4 * (p - 1) + 2 + c + 1)
                        pool.sem_inc(s_pool_turn, 1)
                        pool.tensor_tensor(ot[:, 1 - e, cols], ot[:, 1 - e, cols], ot_lo[:, cols], ALU.add
                                           ).then_inc(s_join, 1)
                    if k in NORM_AT and not first(p):
                        c = NORM_AT[k]
                        cols = ot[:, 1 - e, c * HALF:(c + 1) * HALF].rearrange("p (t i) -> p t i", t=4)
                        pool.wait_ge(s_join, 2 * (p - 1) + c + 1)
                        pool.wait_ge(s_rb, 32 * p)
                        pool.sem_inc(s_pool_turn, 1)
                        pool.tensor_tensor(cols, cols,
                                           rb[:, :].rearrange("p (i t) -> p t i", t=TILES)[:, 4 * c:4 * c + 4, :],
                                           ALU.mult).then_inc(s_norm, 1)

            pairs_of(pool, body)

        @block.scalar
        def _(act):
            def project_hi(q, e, done, n):
                what, c = PROJECTIONS[n]
                bank = ps_x[BANK[1 - e]["project", n]]
                act.wait_ge(s_proj, done + n + 1)
                if what == "v":
                    dst = vs_heads[:, 8 * c:8 * c + 8, 0, :]
                    src = bank[:, :].rearrange("p (x d) -> p x d", d=DH)
                else:
                    if c == 0:
                        at_least(act, s_qs if what == "q" else s_ks, 64 * q)
                    stage = stage_q if what == "q" else stage_k
                    dst, src = stage[:, 0, c * HALF:(c + 1) * HALF], bank[:, :]
                act.activation(dst, src, ACT.Copy)
                at_least(act, s_proj_lo, done + n - 1)
                act.activation(full[n % 2], bank[:, :], ACT.Copy).then_inc(s_proj_full, 1)

            def high_of_tokens(b):
                act.wait_ge(s_xturned, b + 1)
                act.activation(x_part[b][:, 0, :], ps_s[b % 2][:, :], ACT.Copy).then_inc(s_xhi, 1)

            def tokens_with_bias(b):
                act.activation(y[:, b * N:(b + 1) * N], ps_s[b % 2][:, :], ACT.Identity,
                               bias=bo_col[:, 0:1]).then_inc(s_xhi, 1)

            act.wait_ge(s_w0raw, 48)
            act.activation(ws[:, :, 0, :], w_first[:, 0:2 * P].rearrange("p (w n) -> p w n", w=2), ACT.Copy
                           ).then_inc(s_w0hi, 1)
            act.activation(wv[:, 0, :], w_first[:, 2 * P:4 * P], ACT.Copy).then_inc(s_w0hi, 1)
            high_of_tokens(0)
            for n in range(NQK):
                project_hi(0, 0, 0, n)
            act.wait_ge(s_small, 48)
            tokens_with_bias(0)
            for b in range(1, B):
                high_of_tokens(b)
                tokens_with_bias(b)

            def deviations(b, half):
                act.wait_ge(f_mv, TILES * norms_before(b, half) + TILES)
                act.activation(dev[half][:, :], mv[half][:, :, 1], ACT.Sqrt, bias=eps_col[:, 0:1]).then_inc(f_dev, 1)

            def tokens_before(b):
                act.wait_ge(f_x1t, b + 1)
                at_least(act, f_mix, 2 * b)
                act.activation(x1t[:, 1:N + 1], ps_s[1][:, :], ACT.Copy).then_inc(f_x1c, 1)
                act.wait_ge(f_x1c, b + 1)
                at_least(act, f_r, 2 * (b - 1))
                for n, mix in enumerate((mix_r, mix_k)):
                    act.activation(mix[b % 2], x1t[:, 0:N], ACT.Copy, scale=small[:, 2 + n:3 + n]
                                   ).then_inc(f_prev, 1)

            act.wait_ge(f_wt, 1)
            act.activation(ffn_t[:, :, :], ps_o[:, 0:3 * C].rearrange("p (w c) -> p w c", w=3), ACT.Copy
                           ).then_inc(f_wc, 1)

            def exp_of(p, k):
                a, t = divmod(k, TILES)
                if t == 0:
                    at_least(act, s_eps, 2 * (p - 1) + a + 1)
                act.wait_ge(s_masked, SLOTS * p + k + 1)
                cols = tile[:, k % RING, 0:(t + 1) * P]
                act.activation(cols, cols, ACT.Exp, bias=neg_max[:, k % RING:k % RING + 1], scale=-1.0,
                               accum_out=sums[:, a, t:t + 1]).then_inc(s_exp, 1)

            def high_of(p, k, e):
                a, t = divmod(k, TILES)
                for q in range(FIRST_QUAD[t], FIRST_QUAD[t + 1]):
                    _, j, m = QUADS[q]
                    n = a * NQ + q
                    pt, g = (pt0, 0) if t < 4 else (pt1, 1)
                    if q in (0, FIRST_QUAD[4]):
                        at_least(act, s_pv, 4 * p + 2 * a + g - 1)
                    act.wait_ge(s_turned, 2 * NQ * p + n + 1)
                    act.activation(pt[:, 0, j:j + m, (t - 4 * g) * P:(t - 4 * g + 1) * P],
                                   ps_t[BANK[e]["quad", n]][:, 0:m, :], ACT.Copy).then_inc(s_hi, 1)

            def take_values(p, e, a, g):
                if a == 0 and g == 0:
                    at_least(act, s_out, 2 * (p - 1))
                if a == 0:
                    at_least(act, s_join, 2 * (p - 1) + g + 1)
                act.wait_ge(s_pv, 4 * p + 2 * a + g + 1)
                rows, cols = slice(a * DH, (a + 1) * DH), slice(g * HALF, (g + 1) * HALF)
                act.activation(ot[rows, e, cols], ps_o[0:DH, :], ACT.Copy)
                act.activation(ot_lo[rows, cols], ps_o[DH:P, :], ACT.Copy).then_inc(s_ot, 1)

            def body(i, e, p, live):
                for k in range(SLOTS):
                    if live and k - 1 in PROJECT_AT[e]:
                        n = PROJECT_AT[e][k - 1]
                        if not (last(p) and n < NQK):
                            project_hi(p + 1, 1 - e, projected(p, e), n)
                    if k == 0 and not first(p):
                        exp_of(p - 1, SLOTS - 1)
                    if k >= 1 and live:
                        exp_of(p, k - 1)
                    if k < TURN_LAG and not first(p):
                        high_of(p - 1, SLOTS - TURN_LAG + k, e)
                    if k >= TURN_LAG and live:
                        if k == TURN_LAG + 4 and first(p):
                            act.wait_ge(s_wstored, 16 * 6)
                            act.wait_ge(s_xstored, 16 * B)
                        high_of(p, k - TURN_LAG, e)
                    if k in PV_AT:
                        a, g, js, before = PV_AT[k]
                        if js[-1] == 4 * g + 3 and not (before and first(p)) and (before or live):
                            q, par = (p - 1, 1 - e) if before else (p, e)
                            take_values(q, par, a, g)
                    if not live and k == NORM_AHEAD:
                        deviations(0, 0)
                    if not live and k == MIX_AHEAD:
                        act.wait_ge(s_proj_lo, 6 * ALL_PAIRS)
                        tokens_before(0)

            pairs_of(act, body)

            for b in range(1, B + 1):
                if b < B:
                    deviations(b, 0)
                for c in range(2):
                    act.wait_ge(f_k, 2 * (b - 1) + c + 1)
                    act.activation(relu[(b - 1) % 2][:, c * HALF:(c + 1) * HALF], ps_x[c][:, :], ACT.Relu
                                   ).then_inc(f_relu, 1)
                for c, bank in enumerate((ps_x[2], ps_o)):
                    act.wait_ge(f_r, 2 * (b - 1) + c + 1)
                    act.activation(gate[(b - 1) % 2][:, 4 * c:4 * c + 4, :],
                                   bank[:, :].rearrange("p (t c) -> p t c", t=4), ACT.Sigmoid).then_inc(f_sig, 1)
                if b < B:
                    tokens_before(b)
                deviations(b - 1, 1)

        @block.vector
        def _(dve):
            dve.wait_ge(s_w0hi, 2)
            dve.tensor_tensor(ws[:, :, 1, :], w_first[:, 0:2 * P].rearrange("p (w n) -> p w n", w=2),
                              ws[:, :, 0, :].bitcast(F32), ALU.subtract).then_inc(s_w0lo, 1)
            dve.tensor_tensor(wv[:, 1, :], w_first[:, 2 * P:4 * P], wv[:, 0, :].bitcast(F32), ALU.subtract
                              ).then_inc(s_w0lo, 1)

            def low_of_tokens(b):
                hi, lo = (x_part[b][:, h, :] for h in (0, 1))
                dve.wait_ge(s_xhi, 1 if b == 0 else 2 * b + 2)
                dve.tensor_tensor(lo, ps_s[b % 2][:, :], hi.bitcast(F32), ALU.subtract).then_inc(s_xlo, 1)

            low_of_tokens(0)
            dve.wait_ge(s_wraw, 48)
            for w in range(3):
                cols = slice(w * N, (w + 1) * N)
                dve.tensor_copy(w_hi[:, cols], w_raw[w]).then_inc(s_whi, 1)
                dve.wait_ge(s_whi, w + 1)
                dve.tensor_tensor(w_lo[:, cols], w_raw[w], w_hi[:, cols].bitcast(F32), ALU.subtract
                                  ).then_inc(s_wlo, 1)
            second = ot[:, :, P:2 * P]
            dve.wait_ge(s_proj, NQK)
            dve.tensor_copy(ws[:, :, 0, :], second).then_inc(s_w0hi, 1)
            dve.wait_ge(s_w0hi, 3)
            dve.tensor_tensor(ws[:, :, 1, :], second, ws[:, :, 0, :].bitcast(F32), ALU.subtract).then_inc(s_w0lo, 1)
            for b in range(1, B):
                low_of_tokens(b)
            dve.wait_ge(s_small, 48)
            dve.tensor_scalar(small[:, 2:4], small[:, 0:2], -1.0, 1.0, ALU.mult, ALU.add)

            def evacuate(p, k):
                if k >= RING:
                    a, t = divmod(k - RING, TILES)
                    dve.wait_ge(s_turned, 2 * NQ * p + a * NQ + FIRST_QUAD[t + 1])
                else:
                    a, t = divmod(SLOTS + k - RING, TILES)
                    at_least(dve, s_turned, 2 * NQ * (p - 1) + a * NQ + FIRST_QUAD[t + 1])
                dve.wait_ge(s_scores, SLOTS * p + k + 1)
                dve.tensor_scalar(tile[:, k % RING, :], ps_s[k % 2][:, :], -SCALE, None, ALU.mult, ALU.min,
                                  accum_out=neg_max[:, k % RING:k % RING + 1]).then_inc(s_evac, 1)

            def low_of(p, k, e):
                a, t = divmod(k, TILES)
                for q in range(FIRST_QUAD[t], FIRST_QUAD[t + 1]):
                    _, j, m = QUADS[q]
                    n = a * NQ + q
                    pt, g = (pt0, 0) if t < 4 else (pt1, 1)
                    hi, lo = (pt[:, h, j:j + m, (t - 4 * g) * P:(t - 4 * g + 1) * P] for h in (0, 1))
                    dve.wait_ge(s_hi, 2 * NQ * p + n + 1)
                    dve.tensor_tensor(lo, ps_t[BANK[e]["quad", n]][:, 0:m, :], hi.bitcast(F32), ALU.subtract
                                      ).then_inc(s_lo, 1)

            def recips_of(p, a):
                dve.wait_ge(s_exp, SLOTS * p + TILES * (a + 1))
                dve.tensor_scalar(sums_eps[:, a, :], sums[:, a, :], EPS_SUM, None, ALU.add).then_inc(s_eps, 1)
                at_least(dve, s_rdram, 16 * (2 * (p - 1) + a + 1))
                dve.wait_ge(s_eps, 2 * p + a + 1)
                dve.reciprocal(recips[:, a, :], sums_eps[:, a, :]).then_inc(s_recip, 1)

            def add_out(i, e, p, c):
                q = p - 1
                b = q // PAIRS if isinstance(q, int) else ((i - 1) // 4 if e == 0 else i // 4)
                cols = y[:, bass.ds(b * N + c * HALF, HALF)]
                dve.wait_ge(s_out, 2 * q + c + 1)
                dve.tensor_tensor(cols, cols, ps_x[BANK[e]["out", c]][:, :], ALU.add).then_inc(s_yadd, 1)

            def moments(b, half, src):
                done = TILES * norms_before(b, half)
                for t in range(TILES):
                    dve.bn_stats(stats[:, t, :], src[:, t, :]).then_inc(f_stats, 1)
                for t in range(TILES):
                    dve.wait_ge(f_stats, done + t + 1)
                    dve.bn_aggr(mv[half][:, t, :], stats[:, t, :]).then_inc(f_mv, 1)

            def normed(b, half, dst, src, done):
                n = norms_before(b, half) + 1
                dve.wait_ge(f_dev, n)
                dve.reciprocal(rstd[half][:, :], dev[half][:, :]).then_inc(f_rstd, 1)
                dve.wait_ge(f_rstd, n)
                for t in range(TILES):
                    ins = dve.tensor_scalar(dst[:, t, :], src[:, t, :], mv[half][:, t, 0:1], rstd[half][:, t:t + 1],
                                            ALU.subtract, ALU.mult)
                ins.then_inc(done, 1)

            def first_moments(b):
                dve.wait_ge(f_yt, b + 1)
                moments(b, 0, tokens(ps_s[0][:, :]))

            def mixes(b):
                for n, mix in enumerate((mix_r, mix_k)):
                    dve.wait_ge(f_prev, 2 * b + n + 1)
                    dve.scalar_tensor_tensor(out=mix[b % 2], in0=x1t[:, 1:N + 1], scalar=small[:, n:n + 1],
                                             in1=mix[b % 2], op0=ALU.mult, op1=ALU.add).then_inc(f_mix, 1)

            def body(i, e, p, live):
                for k in range(SLOTS):
                    if live:
                        evacuate(p, k)
                    if k == 1 and not first(p):
                        recips_of(p - 1, 1)
                    if k == 9 and live:
                        recips_of(p, 0)
                    if k in OUT_AT and not first(p):
                        add_out(i, e, p, OUT_AT[k])
                    if k < TURN_LAG and not first(p):
                        low_of(p - 1, SLOTS - TURN_LAG + k, e)
                    if k >= TURN_LAG and live:
                        low_of(p, k - TURN_LAG, e)
                    if not live and k == NORM_AHEAD:
                        first_moments(0)
                        normed(0, 0, x1[0], tokens(ps_s[0][:, :]), f_x1)
                    if not live and k == MIX_AHEAD:
                        mixes(0)

            pairs_of(dve, body)

            for b in range(1, B + 1):
                q = (b - 1) % 2
                if b < B:
                    first_moments(b)
                for c in range(2):
                    dve.wait_ge(f_relu, 2 * (b - 1) + c + 1)
                    cols = relu[q][:, c * HALF:(c + 1) * HALF]
                    dve.scalar_tensor_tensor(out=cols, in0=ps_x[c][:, :], scalar=0.0, in1=cols,
                                             op0=ALU.max, op1=ALU.mult).then_inc(f_act, 1)
                if b < B:
                    normed(b, 0, x1[b % 2], tokens(ps_s[0][:, :]), f_x1)
                for c in range(2):
                    dve.wait_ge(f_sig, 2 * (b - 1) + c + 1)
                    dve.wait_ge(f_v, 2 * (b - 1) + c + 1)
                    part = gate[q][:, 4 * c:4 * c + 4, :]
                    dve.tensor_tensor(part, part, ps_x[c][:, :].rearrange("p (t c) -> p t c", t=4), ALU.mult
                                      ).then_inc(f_gate, 1)
                dve.wait_ge(f_gate, 2 * b)
                dve.tensor_tensor(gate[q], gate[q], x1[q], ALU.add).then_inc(f_sum, 1)
                dve.wait_ge(f_sum, b)
                moments(b - 1, 1, gate[q])
                if b < B:
                    mixes(b)
                normed(b - 1, 1, fin[b - 1], gate[q], f_fin)

        @block.tensor
        def _(pe):
            mm = nc.tensor.matmul
            turn = nc.tensor.transpose
            pe.wait_ge(s_ident, 4)

            def turn_tokens(b):
                for t in range(TILES):
                    ins = turn(ps_s[b % 2][:, t * P:(t + 1) * P], tile[:, b, t * P:(t + 1) * P], ident[:, :])
                ins.then_inc(s_xturned, 1)

            pe.wait_ge(s_x0raw, 16)
            turn_tokens(0)

            def drained(p, e, kind, n):
                at = [(u[0], u[2]) for u in SHARED[e]].index((kind, n))
                before = [(p - 1, 1 - e, m) for m in range(len(SHARED[1 - e]))] + [(p, e, m) for m in range(at)]
                for q, f, m in reversed(before):
                    what, k, u = SHARED[f][m]
                    if m % NSHARED != at % NSHARED:
                        continue
                    turned = q - 1 if k < TURN_LAG else q
                    if isinstance(q, int):
                        owner = {"quad": turned, "project": q + 1 if u < NQK else q, "out": q - 1}[what]
                        if q < 0 or not 0 <= owner < ALL_PAIRS:
                            continue
                    if what == "quad":
                        pe.wait_ge(s_lo, 2 * NQ * turned + u + 1)
                    elif what == "project":
                        pe.wait_ge(s_proj_full, projected(q, f) + u + 1)
                    else:
                        pe.wait_ge(s_yadd, 2 * (q - 1) + u + 1)
                    return

            def project(e, n):
                bank = ps_x[BANK[e]["project", n]]
                what, c = PROJECTIONS[n]
                parts = ((0, 0), (1, 0), (0, 1))
                if what == "v":
                    for t in range(2):
                        tokens_of = slice((2 * c + t) * P, (2 * c + t + 1) * P)
                        for m, (wh, xh) in enumerate(parts):
                            ins = mm(bank[:, 2 * t * P:2 * (t + 1) * P], xs[:, xh, tokens_of], wv[:, wh, :],
                                     start=(m == 0), stop=(m == 2))
                else:
                    w = "qk".index(what)
                    for m, (wh, xh) in enumerate(parts):
                        ins = mm(bank[:, :], ws[:, w, wh, :], xs[:, xh, c * HALF:(c + 1) * HALF],
                                 start=(m == 0), stop=(m == 2))
                ins.then_inc(s_proj, 1)

            pe.wait_ge(s_w0lo, 2)
            pe.wait_ge(s_xlo, 1)
            for n in range(NQK):
                for m in range(n):
                    if BANK[1]["project", m] == BANK[1]["project", n]:
                        at_least(pe, s_proj_full, m + 1)
                project(1, n)
            for b in range(1, B):
                if b == 1:
                    pe.wait_ge(s_xraw, 16 * (B - 1))
                if b == 2:
                    pe.wait_ge(s_xhi, 2)
                if b == 3:
                    pe.wait_ge(s_xlo, 2)
                turn_tokens(b)
            pe.wait_ge(f_w, 48)
            for n in range(3):
                ins = turn(ps_o[:, n * C:(n + 1) * C], w_ffn[:, n, :], ident[:, :])
            ins.then_inc(f_wt, 1)
            pe.wait_ge(s_proj_full, NQK)

            def turn_sums(b):
                pe.wait_ge(s_yadd, 2 * PAIRS * (b + 1))
                at_least(pe, f_x1, b)
                for t in range(TILES):
                    ins = turn(ps_s[0][:, t * P:(t + 1) * P], y[:, b * N + t * P:b * N + (t + 1) * P], ident[:, :])
                ins.then_inc(f_yt, 1)

            def turn_normed(b):
                pe.wait_ge(f_x1, b + 1)
                at_least(pe, f_x1c, b)
                for t in range(TILES):
                    ins = turn(ps_s[1][:, t * P:(t + 1) * P], x1[b % 2][:, t, :], ident[:, :])
                ins.then_inc(f_x1t, 1)

            def scores(p, e, k):
                a, t = divmod(k, TILES)
                if k == 0:
                    pe.wait_ge(s_qs, 64 * (p + 1))
                    pe.wait_ge(s_ks, 64 * (p + 1))
                if k < 2 and first(p):
                    pe.wait_ge(s_xlo, B)
                at_least(pe, s_evac, SLOTS * p + k - 1)
                q = qs[:, e, a, t * P:(t + 1) * P]
                for c in range(2):
                    for h in range(2):
                        ins = mm(ps_s[k % 2][:, c * HALF:(c + 1) * HALF], q, ks[:, e, a, h, c * HALF:(c + 1) * HALF],
                                 start=(h == 0), stop=(h == 1))
                ins.then_inc(s_scores, 1)

            def turn_quad(p, k, e, part):
                a, t = divmod(k, TILES)
                if part == 0:
                    pe.wait_ge(s_exp, SLOTS * p + k + 1)
                q = FIRST_QUAD[t] + part
                if q < FIRST_QUAD[t + 1]:
                    _, j, m = QUADS[q]
                    n = a * NQ + q
                    drained(p + (1 if k + TURN_LAG >= SLOTS else 0), e, "quad", n)
                    for b in range(m):
                        ins = turn(ps_t[BANK[e]["quad", n]][:, b, :], tile[:, k % RING, (j + b) * P:(j + b + 1) * P],
                                   ident[:, :])
                    ins.then_inc(s_turned, 1)

            def turn_of_slot(p, k, e, live, part):
                if k < TURN_LAG and not first(p):
                    turn_quad(p - 1, SLOTS - TURN_LAG + k, e, part)
                if k >= TURN_LAG and live:
                    turn_quad(p, k - TURN_LAG, e, part)

            def values(p, e, a, g, js):
                pt = (pt0, pt1)[g]
                if js[0] == 0:
                    pe.wait_ge(s_lo, 2 * NQ * p + a * NQ + FIRST_QUAD[4 * g + 4])
                    at_least(pe, s_ot, 4 * p + 2 * a + g)
                    if first(p) and a == 0 and g == 0:
                        pe.wait_ge(f_wc, 1)
                if e == 0 and a == 0:
                    pe.wait_ge(s_proj_lo, projected(p, 0) + NQK + js[-1] // 2 + 1)
                final = 4 * g + 3
                for j in js:
                    off = max(j - 4 * g, 0) * P
                    for h in range(2):
                        ins = mm(ps_o[:, off:HALF], vs[:, j, e, a, :, :].rearrange("p h d -> p (h d)"),
                                 pt[:, h, j, off:HALF], start=(j == 0 and h == 0), stop=(j == final and h == 1))
                if js[-1] == final:
                    ins.then_inc(s_pv, 1)

            def project_out(p, e, c):
                pe.wait_ge(s_norm, 2 * p + c + 1)
                if c == 0:
                    pe.wait_ge(s_wo, 16 * (p + 1))
                mm(ps_x[BANK[1 - e]["out", c]][:, :], wos[:, :], ot[:, e, c * HALF:(c + 1) * HALF],
                   start=True, stop=True).then_inc(s_out, 1)

            def body(i, e, p, live):
                for k in range(SLOTS):
                    if live:
                        scores(p, e, k)
                    turn_of_slot(p, k, e, live, 0)
                    if k in PV_AT:
                        a, g, js, before = PV_AT[k]
                        if before and not first(p):
                            values(p - 1, 1 - e, a, g, js)
                        if not before and live:
                            values(p, e, a, g, js)
                    turn_of_slot(p, k, e, live, 1)
                    n = PROJECT_AT[e].get(k)
                    if live and n is not None and not (last(p) and n < NQK):
                        if n == 0:
                            if first(p):
                                pe.wait_ge(s_w0lo, 3)
                            at_least(pe, s_ws, 16 * p)
                            if e == 1:
                                pe.wait_ge(s_xs, 16 * (i + 1))
                        if n == NQK:
                            at_least(pe, s_wv, 16 * i)
                        drained(p, e, "project", n)
                        project(e, n)
                    if k in OUT_AT and not first(p):
                        c = OUT_AT[k]
                        drained(p, e, "out", c)
                        project_out(p - 1, 1 - e, c)
                    if not live and k == NORM_AHEAD:
                        pe.wait_ge(s_evac, SLOTS * ALL_PAIRS)
                        turn_sums(0)
                    if not live and k == MIX_AHEAD:
                        turn_normed(0)

            pairs_of(pe, body)

            for b in range(1, B + 1):
                q = (b - 1) % 2
                if b < B:
                    turn_sums(b)
                if b == 1:
                    pe.wait_ge(f_wc, 1)
                    pe.wait_ge(s_lo, 2 * NQ * ALL_PAIRS)
                    pe.wait_ge(s_yadd, 2 * ALL_PAIRS)
                    pe.wait_ge(s_ot, 4 * ALL_PAIRS)
                pe.wait_ge(f_mix, 2 * b)
                at_least(pe, f_gate, 2 * (b - 1))
                for c in range(2):
                    mm(ps_x[c][:, :], ffn_t[:, 1, :], mix_k[q][:, c * HALF:(c + 1) * HALF], start=True, stop=True
                       ).then_inc(f_k, 1)
                at_least(pe, f_sig, 2 * (b - 1))
                for c, bank in enumerate((ps_x[2], ps_o)):
                    for t in range(4):
                        ins = mm(bank[:, t * P:(t + 1) * P], mix_r[q][:, (4 * c + t) * P:(4 * c + t + 1) * P],
                                 ffn_t[:, 0, :], start=True, stop=True)
                    ins.then_inc(f_r, 1)
                for c in range(2):
                    pe.wait_ge(f_act, 2 * (b - 1) + c + 1)
                    for t in range(4):
                        ins = mm(ps_x[c][:, t * P:(t + 1) * P], relu[q][:, (4 * c + t) * P:(4 * c + t + 1) * P],
                                 ffn_t[:, 2, :], start=True, stop=True)
                    ins.then_inc(f_v, 1)
                if b < B:
                    turn_normed(b)


_INS = ["L0_attn_x", "L0_attn_Wq", "L0_attn_Wkv", "L0_attn_Wo", "L0_attn_bo",
        "L0_ffn_W_r", "L0_ffn_W_k", "L0_ffn_W_v", "L0_ffn_mu_r", "L0_ffn_mu_k"]


def kernel(**inputs):
    import numpy as np
    import concourse.bacc as bacc
    from concourse.bass_utils import run_bass_kernel_spmd

    nc = bacc.Bacc("TRN2", target_bir_lowering=False, num_devices=1)
    arrays, args = {}, []
    for name in _INS:
        a = np.ascontiguousarray(inputs[name])
        arrays[f"in_{name}"] = a
        args.append(nc.dram_tensor(f"in_{name}", a.shape, mybir.dt.from_np(a.dtype), kind="ExternalInput").ap())
    out = nc.dram_tensor("out", (B, N, C), F32, kind="ExternalOutput").ap()
    build(nc, *args, out)
    return run_bass_kernel_spmd(nc, [arrays], core_ids=[0]).results[0]["out"]
```
